# Optimizing a Trainium2 kernel written in Bass

```python
import numpy as np
import jax
import jax.numpy as jnp

def _softmax(x, axis=-1):
    return jax.nn.softmax(x, axis=axis)

def _gelu(x):
    return jax.nn.gelu(x, approximate=True)

def _silu(x):
    return jax.nn.silu(x)

def _sigmoid(x):
    return jax.nn.sigmoid(x)

def _layernorm(x, axis=-1, eps=1e-05):
    m = jnp.mean(x, axis=axis, keepdims=True)
    v = jnp.var(x, axis=axis, keepdims=True)
    return (x - m) / jnp.sqrt(v + eps)

def _scatter_add(tgt, idx, src, axis=0):
    return tgt.at[idx].add(src)

def _segment_sum(src, seg, n):
    return jax.ops.segment_sum(src, seg, n)
kernel_name = 'mk_rec_standalone_d1_rec_r8_082f31'

def setup_inputs(seed: int=0):
    np.random.seed(seed)
    _w = jnp.asarray

    def _rec_inputs():
        import jax
        import jax.numpy as jnp
        _rk = jax.random.key(seed)
        r_x = jax.random.randint(jax.random.fold_in(_rk, 1), (512, 10246), 0, 2, jnp.int32)
        return r_x
    r_x = _rec_inputs()

    def _L0_rec_setup():
        import jax, jax.numpy as jnp
        import numpy as np
        B = 2048
        D = 32

        def _mean_bag(multi_hot_f, W):
            out = multi_hot_f @ W.T
            return out / jnp.sum(multi_hot_f, axis=1, keepdims=True)
        key = jax.random.key(seed)
        ks = jax.random.split(key, 16)
        s = 0.02
        inp = {'x': jax.random.randint(ks[0], (B, 10246), 0, 2, dtype=jnp.int64) if jax.config.jax_enable_x64 else jax.random.randint(ks[0], (B, 10246), 0, 2, dtype=jnp.int32), 'emb_rate': jax.random.normal(ks[1], (6, D), jnp.float32) * s, 'W_genre': jax.random.normal(ks[2], (D, 25), jnp.float32) * s, 'W_director': jax.random.normal(ks[3], (D, 2186), jnp.float32) * s, 'W_actor': jax.random.normal(ks[4], (D, 8030), jnp.float32) * s, 'emb_gender': jax.random.normal(ks[5], (2, D), jnp.float32) * s, 'emb_age': jax.random.normal(ks[6], (7, D), jnp.float32) * s, 'emb_occ': jax.random.normal(ks[7], (21, D), jnp.float32) * s, 'emb_area': jax.random.normal(ks[8], (3402, D), jnp.float32) * s, 'W1': jax.random.normal(ks[9], (64, 8 * D), jnp.float32) * s, 'b1': jnp.zeros((64,), jnp.float32), 'W2': jax.random.normal(ks[10], (64, 64), jnp.float32) * s, 'b2': jnp.zeros((64,), jnp.float32), 'Wout': jax.random.normal(ks[11], (1, 64), jnp.float32) * s, 'bout': jnp.zeros((1,), jnp.float32)}
        return inp
    _L0_rec_all = _L0_rec_setup()
    _L0_rec_in = {k: v for k, v in _L0_rec_all.items() if k in ('emb_rate', 'W_genre', 'W_director', 'W_actor', 'emb_gender', 'emb_age', 'emb_occ', 'emb_area', 'W1', 'b1', 'W2', 'b2', 'Wout', 'bout')}
    del _L0_rec_all
    return {'r_x': r_x, 'L0_rec_emb_rate': _L0_rec_in['emb_rate'], 'L0_rec_W_genre': _L0_rec_in['W_genre'], 'L0_rec_W_director': _L0_rec_in['W_director'], 'L0_rec_W_actor': _L0_rec_in['W_actor'], 'L0_rec_emb_gender': _L0_rec_in['emb_gender'], 'L0_rec_emb_age': _L0_rec_in['emb_age'], 'L0_rec_emb_occ': _L0_rec_in['emb_occ'], 'L0_rec_emb_area': _L0_rec_in['emb_area'], 'L0_rec_W1': _L0_rec_in['W1'], 'L0_rec_b1': _L0_rec_in['b1'], 'L0_rec_W2': _L0_rec_in['W2'], 'L0_rec_b2': _L0_rec_in['b2'], 'L0_rec_Wout': _L0_rec_in['Wout'], 'L0_rec_bout': _L0_rec_in['bout']}

def reference(r_x, L0_rec_emb_rate, L0_rec_W_genre, L0_rec_W_director, L0_rec_W_actor, L0_rec_emb_gender, L0_rec_emb_age, L0_rec_emb_occ, L0_rec_emb_area, L0_rec_W1, L0_rec_b1, L0_rec_W2, L0_rec_b2, L0_rec_Wout, L0_rec_bout):
    import jax
    import jax.numpy as jnp

    def _L0_rec_ref(x, emb_rate, W_genre, W_director, W_actor, emb_gender, emb_age, emb_occ, emb_area, W1, b1, W2, b2, Wout, bout):
        import jax, jax.numpy as jnp
        import numpy as np
        B = 2048
        D = 32

        def _mean_bag(multi_hot_f, W):
            out = multi_hot_f @ W.T
            return out / jnp.sum(multi_hot_f, axis=1, keepdims=True)
        rate_idx = x[:, 0]
        genre = x[:, 1:26].astype(jnp.float32)
        director = x[:, 26:2212].astype(jnp.float32)
        actor = x[:, 2212:10242].astype(jnp.float32)
        gender_idx = x[:, 10242]
        age_idx = x[:, 10243]
        occ_idx = x[:, 10244]
        area_idx = x[:, 10245]
        item_emb = jnp.concatenate([emb_rate[rate_idx], _mean_bag(genre, W_genre), _mean_bag(director, W_director), _mean_bag(actor, W_actor)], axis=1)
        user_emb = jnp.concatenate([emb_gender[gender_idx], emb_age[age_idx], emb_occ[occ_idx], emb_area[area_idx]], axis=1)
        h = jnp.concatenate([item_emb, user_emb], axis=1)
        h = jax.nn.relu(h @ W1.T + b1)
        h = jax.nn.relu(h @ W2.T + b2)
        return h @ Wout.T + bout
    y = _L0_rec_ref(r_x, L0_rec_emb_rate, L0_rec_W_genre, L0_rec_W_director, L0_rec_W_actor, L0_rec_emb_gender, L0_rec_emb_age, L0_rec_emb_occ, L0_rec_emb_area, L0_rec_W1, L0_rec_b1, L0_rec_W2, L0_rec_b2, L0_rec_Wout, L0_rec_bout)
    return y

_drawn_inputs = setup_inputs


def setup_inputs(seed=0):
    import zlib

    import numpy as np

    out = dict(_drawn_inputs(seed))
    spreads = {'L0_rec_b1': (0.0, 0.1), 'L0_rec_b2': (0.0, 0.1)}
    factors = {'L0_rec_emb_rate': 5.955,
     'L0_rec_W_genre': 8.0,
     'L0_rec_W_director': 176.995,
     'L0_rec_W_actor': 200.0,
     'L0_rec_emb_gender': 3.702,
     'L0_rec_emb_age': 4.55,
     'L0_rec_emb_occ': 7.127,
     'L0_rec_emb_area': 6.097}
    for name, (base, spread) in spreads.items():
        noise = np.random.default_rng([zlib.crc32(name.encode()), seed]).standard_normal(out[name].shape)
        drawn = base * np.exp(spread * noise) if base else spread * noise
        out[name] = jnp.asarray(drawn.astype(out[name].dtype))
    for name, factor in factors.items():
        out[name] = (out[name] * factor).astype(out[name].dtype)
    return out
```

```python
import concourse.bass as bass
from concourse import mybir
from contextlib import ExitStack

P = 128
BATCH = 512
BLOCKS = BATCH // P
D = 32
HID = 64
BAG = D + 1
Z = HID + 1
GENRE, DIRECTOR, ACTOR = 25, 2186, 8030
AREA_ROWS = 3402
TABLES = (6, 2, 7, 21)
TROWS = sum(TABLES)

DIR_CHUNKS = DIRECTOR // P
DIR_REST = DIRECTOR - DIR_CHUNKS * P
ACT_CHUNKS = -(-ACTOR // P)
CHUNKS = 1 + DIR_CHUNKS + ACT_CHUNKS
GENRE_AT, TABLE_AT = 32, 64

GROUP = 4
SLOTS = 4
LOOPS = 4
LOOPED = LOOPS * SLOTS
TAIL = [4, 4, 4, 2, 1, 1]
assert 1 + GROUP * LOOPED + sum(TAIL) == CHUNKS

COLS = {}
_at = 0
for _name, _n in (("idx", 4), ("tables", P), ("w1_tables", HID), ("w1_area", HID), ("r_genre", Z),
                  ("r_director", Z), ("r_actor", Z), ("w2", HID), ("wout", HID), ("bout", 1)):
    COLS[_name] = (_at, _at + _n)
    _at += _n
PCOLS = _at


def build(nc, x_rows, area_index, weights, params, emb_area, out):
    fp32 = mybir.dt.float32
    int32 = mybir.dt.int32
    ALU = mybir.AluOpType
    ACT = mybir.ActivationFunctionType
    AX = mybir.AxisListType

    with ExitStack() as ctx:
        def sb(name, shape, dt=fp32):
            return ctx.enter_context(nc.sbuf_tensor(name, shape, dt))

        def pb(name, shape):
            return ctx.enter_context(nc.psum_tensor(name, shape, fp32))

        def sem(name):
            return ctx.enter_context(nc.semaphore(name))

        x = sb("x", [P, CHUNKS * BATCH], fp32)
        x_int = x[:, :].bitcast(int32)
        w = sb("w", [P, CHUNKS * BAG])
        par = sb("par", [P, PCOLS])
        ident = sb("ident", [P, P])
        area_raw = sb("area_raw", [P, BLOCKS], int32)
        area_clamped = sb("area_clamped", [P, BLOCKS])
        area_wrap = sb("area_wrap", [P, BLOCKS])
        area_row = sb("area_row", [P, BLOCKS], int32)
        area_emb = sb("area_emb", [P, BLOCKS * D])
        area_t = sb("area_t", [BAG, BATCH])
        clamped = sb("clamped", [P, BATCH])
        is_row = sb("is_row", [P, BATCH])
        onehot = sb("onehot", [P, BATCH])
        table_t = sb("table_t", [P, BATCH])
        genre_sum = sb("genre_sum", [BAG, BATCH])
        director_sum = sb("director_sum", [P, BATCH])
        actor_sum = sb("actor_sum", [P, BATCH])
        recip = sb("recip", [P, 3, BLOCKS])
        h1 = sb("h1", [P, BLOCKS, HID])
        h1_t = sb("h1_t", [Z, BATCH])
        scored = sb("scored", [P, BLOCKS, Z])
        y = sb("y", [P, BLOCKS])

        ps_actor = pb("ps_actor", [P, BATCH])
        ps_director = pb("ps_director", [P, BATCH])
        ps_genre = pb("ps_genre", [P, BATCH])
        ps_table = pb("ps_table", [P, BATCH])
        ps_area = pb("ps_area", [P, BATCH])
        ps_user = pb("ps_user", [P, BLOCKS, P])
        ps_z = pb("ps_z", [P, BLOCKS, P])
        ps_h = [pb("ps_h", [P, 2, P]), ps_genre[:, 0:2 * P].rearrange("p (c n) -> p c n", c=2)]

        def col(name, rows=slice(0, P)):
            a, b = COLS[name]
            return par[rows, a:b]

        area_index_in = sem("area_index_in")
        params_in = sem("params_in")
        weights_in = [sem(f"weights_in{i}") for i in range(3)]
        x_in = [sem(f"x_in{s}") for s in range(SLOTS)]
        tail_in = [sem(f"tail_in{s}") for s in range(len(TAIL))]
        mixed_in = sem("mixed_in")
        x_float = sem("x_float")
        zeroed = sem("zeroed")
        ident_zero = sem("ident_zero")
        ident_ready = sem("ident_ready")
        area_step = sem("area_step")
        area_gathered = sem("area_gathered")
        hot_step = sem("hot_step")
        onehot_ready = sem("onehot_ready")
        table_picked = sem("table_picked")
        table_copied = sem("table_copied")
        area_turned = sem("area_turned")
        area_copied = sem("area_copied")
        user_done = sem("user_done")
        genre_done = sem("genre_done")
        genre_copied = sem("genre_copied")
        director_done = sem("director_done")
        director_copied = sem("director_copied")
        z_done = sem("z_done")
        z_used = sem("z_used")
        recip_done = sem("recip_done")
        h1_ready = sem("h1_ready")
        actor_done = sem("actor_done")
        actor_copied = sem("actor_copied")
        h1_turned = sem("h1_turned")
        h1_copied = sem("h1_copied")
        h2_done = sem("h2_done")
        score_step = sem("score_step")
        out_done = sem("out_done")

        tail_first = [1 + GROUP * LOOPED + sum(TAIL[:i]) for i in range(len(TAIL))]
        W_PARTS = [0, 1 + DIR_CHUNKS, 1 + DIR_CHUNKS + ACT_CHUNKS // 2, CHUNKS]

        block = ctx.enter_context(nc.Block())

        @block.sync
        def _(sync):
            sync.dma_start(x_int[:, 0:BATCH], x_rows[:, 0:BATCH]).then_inc(mixed_in, 16)
            for s in range(SLOTS):
                at = (1 + GROUP * s) * BATCH
                sync.dma_start(x_int[:, at:at + GROUP * BATCH],
                               x_rows[:, at:at + GROUP * BATCH]).then_inc(x_in[s], 16)
            with sync.Fori(1, LOOPS) as k:
                for s in range(SLOTS):
                    sync.wait_ge(x_in[s], k * 16)
                    at = k * (SLOTS * GROUP * BATCH) + (1 + GROUP * s) * BATCH
                    sync.dma_start(x_int[:, bass.ds(at, GROUP * BATCH)],
                                   x_rows[:, bass.ds(at, GROUP * BATCH)]).then_inc(x_in[s], 16)
            for i, n in enumerate(TAIL):
                if i < SLOTS:
                    sync.wait_ge(x_in[i], LOOPS * 16)
                at = tail_first[i] * BATCH
                sync.dma_start(x_int[:, at:at + n * BATCH],
                               x_rows[:, at:at + n * BATCH]).then_inc(tail_in[i], 16)
            sync.wait_ge(score_step, 2)
            sync.dma_start(out, y[:, :]).then_inc(out_done, 16)
            sync.wait_ge(out_done, 16)

        @block.scalar
        def _(act):
            act.dma_start(area_raw[:, :], area_index).then_inc(area_index_in, 16)
            act.dma_start(par[:, :], params).then_inc(params_in, 16)
            for i in range(3):
                a, b = W_PARTS[i] * BAG, W_PARTS[i + 1] * BAG
                act.dma_start(w[:, a:b], weights[:, a:b]).then_inc(weights_in[i], 16)
            act.wait_ge(table_picked, 1)
            nc.scalar.copy(table_t[:, :], ps_table[:, :]).then_inc(table_copied, 1)
            act.wait_ge(genre_done, 1)
            nc.scalar.copy(genre_sum[:, :], ps_genre[0:BAG, :]).then_inc(genre_copied, 1)
            act.wait_ge(area_turned, 1)
            nc.scalar.copy(area_t[0:D, :], ps_area[0:D, :]).then_inc(area_copied, 1)
            act.wait_ge(director_done, 1)
            act.wait_ge(zeroed, 2)
            nc.scalar.copy(director_sum[0:BAG, :], ps_director[0:BAG, :]).then_inc(director_copied, 1)
            nc.scalar.copy(director_sum[64:64 + BAG, :], ps_director[64:64 + BAG, :])\
                .then_inc(director_copied, 1)
            act.wait_ge(actor_done, 1)
            nc.scalar.copy(actor_sum[64:64 + BAG, :], ps_actor[64:64 + BAG, :]).then_inc(actor_copied, 1)
            act.wait_ge(h1_turned, 1)
            nc.scalar.activation(h1_t[0:HID, 0:2 * P], ps_h[0][0:HID, :, :], ACT.Relu).then_inc(h1_copied, 1)

        @block.gpsimd
        def _(pool):
            pool.memset(ident[:, :], 0.0).then_inc(ident_zero, 1)
            pool.wait_ge(ident_zero, 1)
            pool.affine_select(out=ident[:, :], in_=ident[:, :], compare_op=ALU.not_equal, fill=1.0,
                               base=0, pattern=[[-1, P]], channel_multiplier=1).then_inc(ident_ready, 1)
            pool.memset(director_sum[:, :], 0.0).then_inc(zeroed, 1)
            pool.wait_ge(zeroed, 1)
            pool.memset(actor_sum[:, :], 0.0).then_inc(zeroed, 1)
            pool.wait_ge(zeroed, 2)
            pool.memset(area_t[D:D + 1, :], 1.0).then_inc(zeroed, 1)
            pool.wait_ge(zeroed, 3)
            pool.memset(h1_t[HID:HID + 1, :], 1.0).then_inc(zeroed, 1)
            pool.wait_ge(area_step, 3)
            for c in range(BLOCKS):
                pool.indirect_dma_start(area_emb[:, c * D:(c + 1) * D], None, emb_area,
                                        bass.IndirectOffsetOnAxis(ap=area_row[:, c:c + 1], axis=0))\
                    .then_inc(area_gathered, 16)

        @block.vector
        def _(dve):
            dve.wait_ge(area_index_in, 16)
            nc.vector.tensor_scalar(area_clamped[:, :], area_raw[:, :], float(-AREA_ROWS),
                                    float(AREA_ROWS - 1), ALU.max, ALU.min).then_inc(area_step, 1)
            dve.wait_ge(area_step, 1)
            nc.vector.tensor_scalar(area_wrap[:, :], area_clamped[:, :], 0.0, float(AREA_ROWS),
                                    ALU.is_lt, ALU.mult).then_inc(area_step, 1)
            dve.wait_ge(area_step, 2)
            nc.vector.tensor_tensor(area_row[:, :], area_clamped[:, :], area_wrap[:, :],
                                    ALU.add).then_inc(area_step, 1)

            dve.wait_ge(mixed_in, 16)
            nc.vector.tensor_copy(x[:, 0:BATCH], x_int[:, 0:BATCH]).then_inc(x_float, 1)
            dve.wait_ge(params_in, 16)
            dve.wait_ge(x_float, 1)
            rows = slice(TABLE_AT, TABLE_AT + TROWS)
            nc.vector.tensor_scalar(clamped[rows, :], x[rows, 0:BATCH], par[rows, 0:1], par[rows, 1:2],
                                    ALU.max, ALU.min).then_inc(hot_step, 1)
            dve.wait_ge(hot_step, 1)
            nc.vector.tensor_scalar(is_row[rows, :], clamped[rows, :], par[rows, 2:3], None,
                                    ALU.is_equal).then_inc(hot_step, 1)
            dve.wait_ge(hot_step, 2)
            nc.vector.scalar_tensor_tensor(onehot[rows, :], clamped[rows, :], par[rows, 3:4], is_row[rows, :],
                                           ALU.is_equal, ALU.add).then_inc(onehot_ready, 1)

            with dve.Fori(0, LOOPS) as k:
                for s in range(SLOTS):
                    dve.wait_ge(x_in[s], k * 16 + 16)
                    at = k * (SLOTS * GROUP * BATCH) + (1 + GROUP * s) * BATCH
                    nc.vector.tensor_copy(x[:, bass.ds(at, GROUP * BATCH)],
                                          x_int[:, bass.ds(at, GROUP * BATCH)]).then_inc(x_float, 1)

            dve.wait_ge(user_done, 1)
            nc.vector.tensor_copy(h1[:, :, :], ps_user[:, :, 0:HID]).then_inc(h1_ready, 1)

            def add_mean(bag):
                dve.wait_ge(z_done, bag + 1)
                nc.vector.reciprocal(recip[:, bag, :], ps_z[:, :, HID]).then_inc(recip_done, 1)
                dve.wait_ge(recip_done, bag + 1)
                dve.wait_ge(h1_ready, 1 + BLOCKS * bag)
                for c in range(BLOCKS):
                    nc.vector.scalar_tensor_tensor(h1[:, c, :], ps_z[:, c, 0:HID], recip[:, bag, c:c + 1],
                                                   h1[:, c, :], ALU.mult, ALU.add).then_inc(h1_ready, 1)

            add_mean(0)
            add_mean(1)
            for i, n in enumerate(TAIL):
                dve.wait_ge(tail_in[i], 16)
                at = tail_first[i] * BATCH
                nc.vector.tensor_copy(x[:, at:at + n * BATCH], x_int[:, at:at + n * BATCH]).then_inc(x_float, 1)
            nc.vector.tensor_copy(scored[:, :, HID], col("bout").to_broadcast([P, BLOCKS]))

            dve.wait_ge(actor_done, 1)
            dve.wait_ge(zeroed, 2)
            nc.vector.tensor_copy(actor_sum[0:BAG, :], ps_actor[0:BAG, :]).then_inc(actor_copied, 1)
            add_mean(2)
            dve.wait_ge(h1_turned, 2)
            nc.vector.tensor_scalar(h1_t[0:HID, 2 * P:4 * P], ps_h[1][0:HID, :, :], 0.0, None,
                                    ALU.max).then_inc(h1_copied, 1)
            dve.wait_ge(h2_done, 1)
            nc.vector.scalar_tensor_tensor(
                scored[:, :, 0:HID], ps_user[:, :, 0:HID], 0.0,
                col("wout").rearrange("p (a n) -> p a n", a=1).to_broadcast([P, BLOCKS, HID]),
                ALU.max, ALU.mult).then_inc(score_step, 1)
            dve.wait_ge(score_step, 1)
            nc.vector.tensor_reduce(y[:, :], scored[:, :, :], AX.X, ALU.add).then_inc(score_step, 1)

        @block.tensor
        def _(pe):
            def x_chunk(c, rows=slice(0, P)):
                return x[rows, c * BATCH:(c + 1) * BATCH]

            def w_chunk(c, rows=slice(0, P)):
                return w[rows, c * BAG:(c + 1) * BAG]

            def bag_chunk(c):
                half = 64 * (c % 2)
                director = c <= DIR_CHUNKS
                ps = ps_director if director else ps_actor
                first = c == 1 if director else c <= DIR_CHUNKS + 2
                last = c > DIR_CHUNKS - 2 if director else c > CHUNKS - 3
                return nc.tensor.matmul(ps[half:half + BAG, :], w_chunk(c), x_chunk(c), start=first, stop=last)

            pe.wait_ge(weights_in[0], 16)
            pe.wait_ge(x_float, 1)
            rows = slice(GENRE_AT, GENRE_AT + 32)
            nc.tensor.matmul(ps_genre[0:BAG, :], w_chunk(0, rows), x_chunk(0, rows),
                             start=True, stop=True).then_inc(genre_done, 1)
            rows = slice(0, 32)
            nc.tensor.matmul(ps_director[0:BAG, :], w_chunk(0, rows), x_chunk(0, rows), start=True, stop=False)
            pe.wait_ge(onehot_ready, 1)
            pe.wait_ge(params_in, 16)
            rows = slice(TABLE_AT, TABLE_AT + TROWS)
            nc.tensor.matmul(ps_table[:, :], col("tables", rows), onehot[rows, :],
                             start=True, stop=True).then_inc(table_picked, 1)

            def user_part():
                pe.wait_ge(area_gathered, 16 * BLOCKS)
                pe.wait_ge(ident_ready, 1)
                for c in range(BLOCKS):
                    last = nc.tensor.transpose(ps_area[0:D, c * P:(c + 1) * P],
                                               area_emb[:, c * D:(c + 1) * D], ident[:, :])
                last.then_inc(area_turned, 1)

            def user_layer_one():
                pe.wait_ge(area_copied, 1)
                pe.wait_ge(zeroed, 4)
                pe.wait_ge(table_copied, 1)
                for c in range(BLOCKS):
                    cs = slice(c * P, (c + 1) * P)
                    nc.tensor.matmul(ps_user[:, c, 0:HID], area_t[:, cs], col("w1_area", slice(0, BAG)),
                                     start=True, stop=False)
                    last = nc.tensor.matmul(ps_user[:, c, 0:HID], table_t[:, cs], col("w1_tables"),
                                            start=False, stop=True)
                last.then_inc(user_done, 1)

            def bag_layer_one(sums, rows, r):
                for c in range(BLOCKS):
                    last = nc.tensor.matmul(ps_z[:, c, 0:Z], sums[rows, c * P:(c + 1) * P], col(r, rows),
                                            start=True, stop=True)
                last.then_inc(z_done, 1)

            chunk = 1
            for g, n in enumerate([GROUP] * LOOPED + TAIL):
                pe.wait_ge(x_float, g + 2)
                for c in range(chunk, chunk + n):
                    if c in W_PARTS[1:3]:
                        pe.wait_ge(weights_in[W_PARTS.index(c)], 16)
                    last = bag_chunk(c)
                    if c == DIR_CHUNKS:
                        last.then_inc(director_done, 1)
                chunk += n
                if g == 6:
                    user_part()
                if g == 8:
                    user_layer_one()
                if g == 10:
                    pe.wait_ge(genre_copied, 1)
                    bag_layer_one(genre_sum, slice(0, BAG), "r_genre")
                if g == 15:
                    pe.wait_ge(director_copied, 2)
                    pe.wait_ge(h1_ready, 1 + BLOCKS)
                    bag_layer_one(director_sum, slice(0, 64 + BAG), "r_director")
            last.then_inc(actor_done, 1)

            pe.wait_ge(actor_copied, 2)
            pe.wait_ge(h1_ready, 1 + 2 * BLOCKS)
            bag_layer_one(actor_sum, slice(0, 64 + BAG), "r_actor")
            for c in range(BLOCKS):
                pe.wait_ge(h1_ready, 1 + 2 * BLOCKS + c + 1)
                last = nc.tensor.transpose(ps_h[c // 2][0:HID, c % 2, :], h1[:, c, :], ident[:, :])
                if c % 2:
                    last.then_inc(h1_turned, 1)
            pe.wait_ge(h1_copied, 2)
            for c in range(BLOCKS):
                last = nc.tensor.matmul(ps_user[:, c, 0:HID], h1_t[:, c * P:(c + 1) * P], col("w2", slice(0, Z)),
                                        start=True, stop=True)
            last.then_inc(h2_done, 1)


def kernel(r_x, L0_rec_emb_rate, L0_rec_W_genre, L0_rec_W_director, L0_rec_W_actor, L0_rec_emb_gender,
           L0_rec_emb_age, L0_rec_emb_occ, L0_rec_emb_area, L0_rec_W1, L0_rec_b1, L0_rec_W2, L0_rec_b2,
           L0_rec_Wout, L0_rec_bout):
    import numpy as np
    import concourse.bacc as bacc
    from concourse import mybir
    from concourse.bass_utils import run_bass_kernel_spmd

    x = np.asarray(r_x)
    W1, W2 = np.asarray(L0_rec_W1), np.asarray(L0_rec_W2)
    xt = x.reshape(P, BLOCKS, x.shape[1]).transpose(2, 1, 0).reshape(x.shape[1], BATCH)
    d0, a0, u0 = 1 + GENRE, 1 + GENRE + DIRECTOR, 1 + GENRE + DIRECTOR + ACTOR

    rows = np.zeros((CHUNKS * P, BATCH), x.dtype)
    rows[0:DIR_REST] = xt[d0 + DIR_CHUNKS * P:a0]
    rows[GENRE_AT:GENRE_AT + GENRE] = xt[1:d0]
    at = TABLE_AT
    for n, source in zip(TABLES, (0, u0, u0 + 1, u0 + 2)):
        rows[at:at + n] = xt[source]
        at += n
    rows[P:P + DIR_CHUNKS * P] = xt[d0:d0 + DIR_CHUNKS * P]
    rows[P + DIR_CHUNKS * P:P + DIR_CHUNKS * P + ACTOR] = xt[a0:u0]
    x_rows = np.ascontiguousarray(rows.reshape(CHUNKS, P, BATCH).transpose(1, 0, 2)).reshape(P, CHUNKS * BATCH)

    wt = np.zeros((CHUNKS * P, BAG), W1.dtype)
    wt[:, D] = 1.0
    wd = np.asarray(L0_rec_W_director).T
    wt[0:DIR_REST, 0:D] = wd[DIR_CHUNKS * P:]
    wt[GENRE_AT:GENRE_AT + GENRE, 0:D] = np.asarray(L0_rec_W_genre).T
    wt[P:P + DIR_CHUNKS * P, 0:D] = wd[0:DIR_CHUNKS * P]
    wt[P + DIR_CHUNKS * P:P + DIR_CHUNKS * P + ACTOR, 0:D] = np.asarray(L0_rec_W_actor).T
    weights = np.ascontiguousarray(wt.reshape(CHUNKS, P, BAG).transpose(1, 0, 2)).reshape(P, CHUNKS * BAG)

    params = np.zeros((P, PCOLS), W1.dtype)

    def put(name, row, block):
        a = COLS[name][0]
        params[row:row + block.shape[0], a:a + block.shape[1]] = block

    tables = (L0_rec_emb_rate, L0_rec_emb_gender, L0_rec_emb_age, L0_rec_emb_occ)
    w1_at = (0, 4 * D, 5 * D, 6 * D)
    row = TABLE_AT
    for t, n in enumerate(TABLES):
        for j in range(n):
            params[row + j, 0:4] = (-n, n - 1, j, j - n)
        params[row:row + n, COLS["tables"][0] + t * D:COLS["tables"][0] + (t + 1) * D] = np.asarray(tables[t])
        put("w1_tables", t * D, W1[:, w1_at[t]:w1_at[t] + D].T)
        row += n
    put("w1_area", 0, W1[:, 7 * D:8 * D].T)
    put("w1_area", D, np.asarray(L0_rec_b1).reshape(1, HID))
    for name, block, halves in (("r_genre", 1, (0,)), ("r_director", 2, (0, 64)), ("r_actor", 3, (0, 64))):
        for half in halves:
            put(name, half, W1[:, block * D:(block + 1) * D].T)
            params[half + D, COLS[name][0] + HID] = 1.0
    put("w2", 0, W2.T)
    put("w2", HID, np.asarray(L0_rec_b2).reshape(1, HID))
    params[:, COLS["wout"][0]:COLS["wout"][1]] = np.asarray(L0_rec_Wout)
    params[:, COLS["bout"][0]] = np.asarray(L0_rec_bout)

    arrays = {
        "x_rows": x_rows,
        "area_index": np.ascontiguousarray(x[:, u0 + 3].reshape(P, BLOCKS)),
        "weights": weights,
        "params": params,
        "emb_area": np.ascontiguousarray(np.asarray(L0_rec_emb_area)),
    }
    nc = bacc.Bacc("TRN2", target_bir_lowering=False, num_devices=1)
    args = [nc.dram_tensor(name, a.shape, mybir.dt.from_np(a.dtype), kind="ExternalInput").ap()
            for name, a in arrays.items()]
    out = nc.dram_tensor("out", (P, BLOCKS), mybir.dt.float32, kind="ExternalOutput").ap()
    build(nc, *args, out)
    got = run_bass_kernel_spmd(nc, [arrays], core_ids=[0]).results[0]["out"]
    return got.reshape(BATCH, 1)
```

```python
import concourse.bass as bass
from concourse import mybir
from contextlib import ExitStack

P = 128
BATCH = 512
BLOCKS = BATCH // P
D = 32
HID = 64
BAG = D + 1
Z = HID + 1
GENRE, DIRECTOR, ACTOR = 25, 2186, 8030
AREA_ROWS = 3402
TABLES = (6, 2, 7, 21)
TROWS = sum(TABLES)

DIR_CHUNKS = DIRECTOR // P
DIR_REST = DIRECTOR - DIR_CHUNKS * P
ACT_CHUNKS = -(-ACTOR // P)
CHUNKS = 1 + DIR_CHUNKS + ACT_CHUNKS
GENRE_AT, TABLE_AT = 32, 64

GROUP = 4
PAIR = 2
SLOTS = 4
LOOPS = 4
LOOPED = LOOPS * SLOTS
TAIL = [4, 4, 4, 2, 1, 1]
assert 1 + GROUP * LOOPED + sum(TAIL) == CHUNKS
LAST_ROWS = 96
assert ACTOR - (ACT_CHUNKS - 1) * P <= LAST_ROWS
HALVES = 2
HALF = BATCH // HALVES
HB = BLOCKS // HALVES

COLS = {}
_at = 0
for _name, _n in (("idx", 4), ("tables", P), ("w1_tables", HID), ("w1_area", HID), ("r_genre", Z),
                  ("r_director", Z), ("r_actor", Z), ("w2", HID), ("wout", HID), ("bout", 1)):
    COLS[_name] = (_at, _at + _n)
    _at += _n
PCOLS = _at


def build(nc, x_rows, area_index, weights, params, emb_area, out):
    fp32 = mybir.dt.float32
    int32 = mybir.dt.int32
    ALU = mybir.AluOpType
    ACT = mybir.ActivationFunctionType
    AX = mybir.AxisListType

    with ExitStack() as ctx:
        def sb(name, shape, dt=fp32):
            return ctx.enter_context(nc.sbuf_tensor(name, shape, dt))

        def pb(name, shape):
            return ctx.enter_context(nc.psum_tensor(name, shape, fp32))

        def sem(name):
            return ctx.enter_context(nc.semaphore(name))

        x = sb("x", [P, CHUNKS * BATCH], fp32)
        x_int = x[:, :].bitcast(int32)
        w = sb("w", [P, CHUNKS * BAG])
        par = sb("par", [P, PCOLS])
        ident = sb("ident", [P, P])
        area_raw = sb("area_raw", [P, BLOCKS], int32)
        area_clamped = sb("area_clamped", [P, BLOCKS])
        area_wrap = sb("area_wrap", [P, BLOCKS])
        area_row = sb("area_row", [P, BLOCKS], int32)
        area_emb = sb("area_emb", [P, BLOCKS * D])
        area_t = sb("area_t", [BAG, BATCH])
        clamped = sb("clamped", [P, BATCH])
        is_row = sb("is_row", [P, BATCH])
        onehot = sb("onehot", [P, BATCH])
        table_t = sb("table_t", [P, BATCH])
        genre_sum = sb("genre_sum", [BAG, BATCH])
        director_sum = sb("director_sum", [P, BATCH])
        actor_sum = sb("actor_sum", [P, BATCH])
        recip = sb("recip", [P, 3, BLOCKS])
        h1 = sb("h1", [P, BLOCKS, HID])
        h1_t = sb("h1_t", [Z, BATCH])
        scored = sb("scored", [P, BLOCKS, Z])
        y = sb("y", [P, BLOCKS])

        ps_actor = pb("ps_actor", [P, BATCH])
        ps_director = pb("ps_director", [P, BATCH])
        ps_genre = pb("ps_genre", [P, BATCH])
        ps_table = pb("ps_table", [P, BATCH])
        ps_area = pb("ps_area", [P, BATCH])
        ps_user = pb("ps_user", [P, BLOCKS, P])
        ps_z = [pb(f"ps_z{h}", [P, HB, P]) for h in range(HALVES)]
        ps_h1 = [t[:, 0:HALF].rearrange("p (c n) -> p c n", c=HB) for t in (ps_table, ps_area)]
        ps_h2 = [ps_genre[:, 0:HALF].rearrange("p (c n) -> p c n", c=HB), ps_user[:, 0:HB, :]]

        def col(name, rows=slice(0, P)):
            a, b = COLS[name]
            return par[rows, a:b]

        area_index_in = sem("area_index_in")
        params_in = sem("params_in")
        weights_in = [sem(f"weights_in{i}") for i in range(3)]
        x_in = [sem(f"x_in{s}") for s in range(SLOTS)]
        tail_in = [sem(f"tail_in{s}") for s in range(len(TAIL))]
        mixed_in = sem("mixed_in")
        x_float = sem("x_float")
        zeroed = sem("zeroed")
        ident_zero = sem("ident_zero")
        ident_ready = sem("ident_ready")
        area_step = sem("area_step")
        area_gathered = sem("area_gathered")
        hot_step = sem("hot_step")
        onehot_ready = sem("onehot_ready")
        table_picked = sem("table_picked")
        table_copied = sem("table_copied")
        area_turned = sem("area_turned")
        area_copied = sem("area_copied")
        user_done = sem("user_done")
        genre_done = sem("genre_done")
        genre_copied = sem("genre_copied")
        director_done = sem("director_done")
        director_copied = sem("director_copied")
        z_done = sem("z_done")
        z_used = sem("z_used")
        recip_done = sem("recip_done")
        h1_ready = sem("h1_ready")
        actor_done = sem("actor_done")
        actor_copied = [sem(f"actor_copied{h}") for h in range(HALVES)]
        h1_turned = sem("h1_turned")
        h1_copied = sem("h1_copied")
        h2_done = sem("h2_done")
        score_step = sem("score_step")
        out_done = sem("out_done")

        tail_first = [1 + GROUP * LOOPED + sum(TAIL[:i]) for i in range(len(TAIL))]
        W_PARTS = [0, 1 + DIR_CHUNKS, 1 + DIR_CHUNKS + ACT_CHUNKS // 2, CHUNKS]

        block = ctx.enter_context(nc.Block())

        @block.sync
        def _(sync):
            sync.dma_start(x_int[:, 0:BATCH], x_rows[:, 0:BATCH]).then_inc(mixed_in, 16)
            for s in range(SLOTS):
                at = (1 + GROUP * s) * BATCH
                sync.dma_start(x_int[:, at:at + GROUP * BATCH],
                               x_rows[:, at:at + GROUP * BATCH]).then_inc(x_in[s], 16)
            with sync.Fori(1, LOOPS) as k:
                for s in range(SLOTS):
                    sync.wait_ge(x_in[s], k * 16)
                    at = k * (SLOTS * GROUP * BATCH) + (1 + GROUP * s) * BATCH
                    sync.dma_start(x_int[:, bass.ds(at, GROUP * BATCH)],
                                   x_rows[:, bass.ds(at, GROUP * BATCH)]).then_inc(x_in[s], 16)
            for i, n in enumerate(TAIL):
                if i < SLOTS:
                    sync.wait_ge(x_in[i], LOOPS * 16)
                at = tail_first[i] * BATCH
                rows = LAST_ROWS if i == len(TAIL) - 1 else P
                sync.dma_start(x_int[0:rows, at:at + n * BATCH],
                               x_rows[0:rows, at:at + n * BATCH]).then_inc(tail_in[i], 16)
            sync.wait_ge(score_step, 2 * HALVES)
            sync.dma_start(out, y[:, :]).then_inc(out_done, 16)
            sync.wait_ge(out_done, 16)

        @block.scalar
        def _(act):
            act.dma_start(area_raw[:, :], area_index).then_inc(area_index_in, 16)
            act.dma_start(par[:, :], params).then_inc(params_in, 16)
            for i in range(3):
                a, b = W_PARTS[i] * BAG, W_PARTS[i + 1] * BAG
                act.dma_start(w[:, a:b], weights[:, a:b]).then_inc(weights_in[i], 16)
            act.wait_ge(table_picked, 1)
            nc.scalar.copy(table_t[:, :], ps_table[:, :]).then_inc(table_copied, 1)
            act.wait_ge(genre_done, 1)
            nc.scalar.copy(genre_sum[:, :], ps_genre[0:BAG, :]).then_inc(genre_copied, 1)
            act.wait_ge(area_turned, 1)
            nc.scalar.copy(area_t[0:D, :], ps_area[0:D, :]).then_inc(area_copied, 1)
            act.wait_ge(director_done, 1)
            act.wait_ge(zeroed, 2)
            nc.scalar.copy(director_sum[0:BAG, :], ps_director[0:BAG, :]).then_inc(director_copied, 1)
            nc.scalar.copy(director_sum[64:64 + BAG, :], ps_director[64:64 + BAG, :])\
                .then_inc(director_copied, 1)
            act.wait_ge(actor_done, 1)
            for h in range(HALVES):
                cs = slice(h * HALF, (h + 1) * HALF)
                nc.scalar.copy(actor_sum[64:64 + BAG, cs], ps_actor[64:64 + BAG, cs]).then_inc(actor_copied[h], 1)
            for h in range(HALVES):
                act.wait_ge(h1_turned, h + 1)
                nc.scalar.activation(h1_t[0:HID, h * HALF:(h + 1) * HALF], ps_h1[h][0:HID, :, :],
                                     ACT.Relu).then_inc(h1_copied, 1)

        @block.gpsimd
        def _(pool):
            pool.memset(ident[:, :], 0.0).then_inc(ident_zero, 1)
            pool.wait_ge(ident_zero, 1)
            pool.affine_select(out=ident[:, :], in_=ident[:, :], compare_op=ALU.not_equal, fill=1.0,
                               base=0, pattern=[[-1, P]], channel_multiplier=1).then_inc(ident_ready, 1)
            pool.memset(director_sum[:, :], 0.0).then_inc(zeroed, 1)
            pool.wait_ge(zeroed, 1)
            pool.memset(actor_sum[:, :], 0.0).then_inc(zeroed, 1)
            pool.wait_ge(zeroed, 2)
            pool.memset(area_t[D:D + 1, :], 1.0).then_inc(zeroed, 1)
            pool.wait_ge(zeroed, 3)
            pool.memset(h1_t[HID:HID + 1, :], 1.0).then_inc(zeroed, 1)
            pool.wait_ge(area_step, 3)
            for c in range(BLOCKS):
                pool.indirect_dma_start(area_emb[:, c * D:(c + 1) * D], None, emb_area,
                                        bass.IndirectOffsetOnAxis(ap=area_row[:, c:c + 1], axis=0))\
                    .then_inc(area_gathered, 16)

        @block.vector
        def _(dve):
            dve.wait_ge(area_index_in, 16)
            nc.vector.tensor_scalar(area_clamped[:, :], area_raw[:, :], float(-AREA_ROWS),
                                    float(AREA_ROWS - 1), ALU.max, ALU.min).then_inc(area_step, 1)
            dve.wait_ge(area_step, 1)
            nc.vector.tensor_scalar(area_wrap[:, :], area_clamped[:, :], 0.0, float(AREA_ROWS),
                                    ALU.is_lt, ALU.mult).then_inc(area_step, 1)
            dve.wait_ge(area_step, 2)
            nc.vector.tensor_tensor(area_row[:, :], area_clamped[:, :], area_wrap[:, :],
                                    ALU.add).then_inc(area_step, 1)

            dve.wait_ge(mixed_in, 16)
            nc.vector.tensor_copy(x[:, 0:BATCH], x_int[:, 0:BATCH]).then_inc(x_float, 1)
            dve.wait_ge(params_in, 16)
            dve.wait_ge(x_float, 1)
            rows = slice(TABLE_AT, TABLE_AT + TROWS)
            nc.vector.tensor_scalar(clamped[rows, :], x[rows, 0:BATCH], par[rows, 0:1], par[rows, 1:2],
                                    ALU.max, ALU.min).then_inc(hot_step, 1)
            dve.wait_ge(hot_step, 1)
            nc.vector.tensor_scalar(is_row[rows, :], clamped[rows, :], par[rows, 2:3], None,
                                    ALU.is_equal).then_inc(hot_step, 1)
            dve.wait_ge(hot_step, 2)
            nc.vector.scalar_tensor_tensor(onehot[rows, :], clamped[rows, :], par[rows, 3:4], is_row[rows, :],
                                           ALU.is_equal, ALU.add).then_inc(onehot_ready, 1)

            with dve.Fori(0, LOOPS) as k:
                for s in range(SLOTS):
                    dve.wait_ge(x_in[s], k * 16 + 16)
                    for j in range(GROUP // PAIR):
                        at = k * (SLOTS * GROUP * BATCH) + (1 + GROUP * s + PAIR * j) * BATCH
                        nc.vector.tensor_copy(x[:, bass.ds(at, PAIR * BATCH)],
                                              x_int[:, bass.ds(at, PAIR * BATCH)]).then_inc(x_float, 1)

            dve.wait_ge(user_done, 1)
            nc.vector.tensor_copy(h1[:, :, :], ps_user[:, :, 0:HID]).then_inc(h1_ready, 1)

            def add_mean(bag, h):
                dve.wait_ge(z_done, HALVES * bag + h + 1)
                nc.vector.reciprocal(recip[:, bag, h * HB:(h + 1) * HB], ps_z[h][:, :, HID]).then_inc(recip_done, 1)
                dve.wait_ge(recip_done, HALVES * bag + h + 1)
                if bag:
                    dve.wait_ge(h1_ready, 1 + BLOCKS * (bag - 1) + HB * (h + 1))
                else:
                    dve.wait_ge(h1_ready, 1)
                for c in range(HB):
                    block = h * HB + c
                    nc.vector.scalar_tensor_tensor(h1[:, block, :], ps_z[h][:, c, 0:HID],
                                                   recip[:, bag, block:block + 1], h1[:, block, :],
                                                   ALU.mult, ALU.add).then_inc(h1_ready, 1)

            for bag in range(2):
                for h in range(HALVES):
                    add_mean(bag, h)
            for i, n in enumerate(TAIL):
                dve.wait_ge(tail_in[i], 16)
                at = tail_first[i] * BATCH
                rows = LAST_ROWS if i == len(TAIL) - 1 else P
                step = PAIR * BATCH if n >= PAIR else HALF
                for a in range(at, at + n * BATCH, step):
                    nc.vector.tensor_copy(x[0:rows, a:a + step], x_int[0:rows, a:a + step]).then_inc(x_float, 1)
            nc.vector.tensor_copy(scored[:, :, HID], col("bout").to_broadcast([P, BLOCKS]))

            dve.wait_ge(actor_done, 1)
            dve.wait_ge(zeroed, 2)
            for h in range(HALVES):
                cs = slice(h * HALF, (h + 1) * HALF)
                nc.vector.tensor_copy(actor_sum[0:BAG, cs], ps_actor[0:BAG, cs]).then_inc(actor_copied[h], 1)
            for h in range(HALVES):
                add_mean(2, h)
            for h in range(HALVES):
                blocks = slice(h * HB, (h + 1) * HB)
                dve.wait_ge(h2_done, h + 1)
                nc.vector.scalar_tensor_tensor(
                    scored[:, blocks, 0:HID], ps_h2[h][:, :, 0:HID], 0.0,
                    col("wout").rearrange("p (a n) -> p a n", a=1).to_broadcast([P, HB, HID]),
                    ALU.max, ALU.mult).then_inc(score_step, 1)
                dve.wait_ge(score_step, 2 * h + 1)
                nc.vector.tensor_reduce(y[:, blocks], scored[:, blocks, :], AX.X, ALU.add).then_inc(score_step, 1)

        @block.tensor
        def _(pe):
            def x_chunk(c, rows=slice(0, P)):
                return x[rows, c * BATCH:(c + 1) * BATCH]

            def w_chunk(c, rows=slice(0, P)):
                return w[rows, c * BAG:(c + 1) * BAG]

            def bag_chunk(c):
                half = 64 * (c % 2)
                director = c <= DIR_CHUNKS
                ps = ps_director if director else ps_actor
                first = c == 1 if director else c <= DIR_CHUNKS + 2
                last = director and c > DIR_CHUNKS - 2
                return nc.tensor.matmul(ps[half:half + BAG, :], w_chunk(c), x_chunk(c), start=first, stop=last)

            pe.wait_ge(weights_in[0], 16)
            pe.wait_ge(x_float, 1)
            rows = slice(GENRE_AT, GENRE_AT + 32)
            nc.tensor.matmul(ps_genre[0:BAG, :], w_chunk(0, rows), x_chunk(0, rows),
                             start=True, stop=True).then_inc(genre_done, 1)
            rows = slice(0, 32)
            nc.tensor.matmul(ps_director[0:BAG, :], w_chunk(0, rows), x_chunk(0, rows), start=True, stop=False)
            pe.wait_ge(onehot_ready, 1)
            pe.wait_ge(params_in, 16)
            rows = slice(TABLE_AT, TABLE_AT + TROWS)
            nc.tensor.matmul(ps_table[:, :], col("tables", rows), onehot[rows, :],
                             start=True, stop=True).then_inc(table_picked, 1)

            def user_part():
                pe.wait_ge(area_gathered, 16 * BLOCKS)
                pe.wait_ge(ident_ready, 1)
                for c in range(BLOCKS):
                    last = nc.tensor.transpose(ps_area[0:D, c * P:(c + 1) * P],
                                               area_emb[:, c * D:(c + 1) * D], ident[:, :])
                last.then_inc(area_turned, 1)

            def user_layer_one():
                pe.wait_ge(area_copied, 1)
                pe.wait_ge(zeroed, 4)
                pe.wait_ge(table_copied, 1)
                for c in range(BLOCKS):
                    cs = slice(c * P, (c + 1) * P)
                    nc.tensor.matmul(ps_user[:, c, 0:HID], area_t[:, cs], col("w1_area", slice(0, BAG)),
                                     start=True, stop=False)
                    last = nc.tensor.matmul(ps_user[:, c, 0:HID], table_t[:, cs], col("w1_tables"),
                                            start=False, stop=True)
                last.then_inc(user_done, 1)

            def bag_layer_one(h, sums, rows, r):
                for c in range(HB):
                    at = h * HALF + c * P
                    last = nc.tensor.matmul(ps_z[h][:, c, 0:Z], sums[rows, at:at + P], col(r, rows),
                                            start=True, stop=True)
                last.then_inc(z_done, 1)

            for c in range(1, CHUNKS - 2, PAIR):
                pair = c // PAIR
                pe.wait_ge(x_float, pair + 2)
                for c in range(c, c + PAIR):
                    if c in W_PARTS[1:3]:
                        pe.wait_ge(weights_in[W_PARTS.index(c)], 16)
                    last = bag_chunk(c)
                    if c == DIR_CHUNKS:
                        last.then_inc(director_done, 1)
                if pair == 13:
                    user_part()
                if pair == 17:
                    user_layer_one()
                if pair == 21:
                    pe.wait_ge(genre_copied, 1)
                    for h in range(HALVES):
                        bag_layer_one(h, genre_sum, slice(0, BAG), "r_genre")
                if pair == 30:
                    pe.wait_ge(director_copied, 2)
                    for h in range(HALVES):
                        pe.wait_ge(h1_ready, 1 + HB * (h + 1))
                        bag_layer_one(h, director_sum, slice(0, 64 + BAG), "r_director")
            for c in range(CHUNKS - 2, CHUNKS):
                rows = slice(0, LAST_ROWS if c == CHUNKS - 1 else P)
                for h in range(HALVES):
                    pe.wait_ge(x_float, (CHUNKS - 3) // PAIR + 2 + (c - CHUNKS + 2) * HALVES + h)
                    cs = slice(h * HALF, (h + 1) * HALF)
                    last = nc.tensor.matmul(ps_actor[64 * h:64 * h + BAG, cs], w_chunk(c, rows),
                                            x_chunk(c, rows)[:, cs], start=False, stop=c == CHUNKS - 1)
            last.then_inc(actor_done, 1)

            for h in range(HALVES):
                pe.wait_ge(actor_copied[h], 2)
                pe.wait_ge(h1_ready, 1 + BLOCKS + HB * (h + 1))
                bag_layer_one(h, actor_sum, slice(0, 64 + BAG), "r_actor")
            for h in range(HALVES):
                for c in range(HB):
                    block = h * HB + c
                    pe.wait_ge(h1_ready, 1 + 2 * BLOCKS + block + 1)
                    last = nc.tensor.transpose(ps_h1[h][0:HID, c, :], h1[:, block, :], ident[:, :])
                last.then_inc(h1_turned, 1)
            for h in range(HALVES):
                pe.wait_ge(h1_copied, h + 1)
                for c in range(HB):
                    at = h * HALF + c * P
                    last = nc.tensor.matmul(ps_h2[h][:, c, 0:HID], h1_t[:, at:at + P], col("w2", slice(0, Z)),
                                            start=True, stop=True)
                last.then_inc(h2_done, 1)


def kernel(r_x, L0_rec_emb_rate, L0_rec_W_genre, L0_rec_W_director, L0_rec_W_actor, L0_rec_emb_gender,
           L0_rec_emb_age, L0_rec_emb_occ, L0_rec_emb_area, L0_rec_W1, L0_rec_b1, L0_rec_W2, L0_rec_b2,
           L0_rec_Wout, L0_rec_bout):
    import numpy as np
    import concourse.bacc as bacc
    from concourse import mybir
    from concourse.bass_utils import run_bass_kernel_spmd

    x = np.asarray(r_x)
    W1, W2 = np.asarray(L0_rec_W1), np.asarray(L0_rec_W2)
    xt = x.reshape(P, BLOCKS, x.shape[1]).transpose(2, 1, 0).reshape(x.shape[1], BATCH)
    d0, a0, u0 = 1 + GENRE, 1 + GENRE + DIRECTOR, 1 + GENRE + DIRECTOR + ACTOR

    rows = np.zeros((CHUNKS * P, BATCH), x.dtype)
    rows[0:DIR_REST] = xt[d0 + DIR_CHUNKS * P:a0]
    rows[GENRE_AT:GENRE_AT + GENRE] = xt[1:d0]
    at = TABLE_AT
    for n, source in zip(TABLES, (0, u0, u0 + 1, u0 + 2)):
        rows[at:at + n] = xt[source]
        at += n
    rows[P:P + DIR_CHUNKS * P] = xt[d0:d0 + DIR_CHUNKS * P]
    rows[P + DIR_CHUNKS * P:P + DIR_CHUNKS * P + ACTOR] = xt[a0:u0]
    x_rows = np.ascontiguousarray(rows.reshape(CHUNKS, P, BATCH).transpose(1, 0, 2)).reshape(P, CHUNKS * BATCH)

    wt = np.zeros((CHUNKS * P, BAG), W1.dtype)
    wt[:, D] = 1.0
    wd = np.asarray(L0_rec_W_director).T
    wt[0:DIR_REST, 0:D] = wd[DIR_CHUNKS * P:]
    wt[GENRE_AT:GENRE_AT + GENRE, 0:D] = np.asarray(L0_rec_W_genre).T
    wt[P:P + DIR_CHUNKS * P, 0:D] = wd[0:DIR_CHUNKS * P]
    wt[P + DIR_CHUNKS * P:P + DIR_CHUNKS * P + ACTOR, 0:D] = np.asarray(L0_rec_W_actor).T
    weights = np.ascontiguousarray(wt.reshape(CHUNKS, P, BAG).transpose(1, 0, 2)).reshape(P, CHUNKS * BAG)

    params = np.zeros((P, PCOLS), W1.dtype)

    def put(name, row, block):
        a = COLS[name][0]
        params[row:row + block.shape[0], a:a + block.shape[1]] = block

    tables = (L0_rec_emb_rate, L0_rec_emb_gender, L0_rec_emb_age, L0_rec_emb_occ)
    w1_at = (0, 4 * D, 5 * D, 6 * D)
    row = TABLE_AT
    for t, n in enumerate(TABLES):
        for j in range(n):
            params[row + j, 0:4] = (-n, n - 1, j, j - n)
        params[row:row + n, COLS["tables"][0] + t * D:COLS["tables"][0] + (t + 1) * D] = np.asarray(tables[t])
        put("w1_tables", t * D, W1[:, w1_at[t]:w1_at[t] + D].T)
        row += n
    put("w1_area", 0, W1[:, 7 * D:8 * D].T)
    put("w1_area", D, np.asarray(L0_rec_b1).reshape(1, HID))
    for name, block, halves in (("r_genre", 1, (0,)), ("r_director", 2, (0, 64)), ("r_actor", 3, (0, 64))):
        for half in halves:
            put(name, half, W1[:, block * D:(block + 1) * D].T)
            params[half + D, COLS[name][0] + HID] = 1.0
    put("w2", 0, W2.T)
    put("w2", HID, np.asarray(L0_rec_b2).reshape(1, HID))
    params[:, COLS["wout"][0]:COLS["wout"][1]] = np.asarray(L0_rec_Wout)
    params[:, COLS["bout"][0]] = np.asarray(L0_rec_bout)

    arrays = {
        "x_rows": x_rows,
        "area_index": np.ascontiguousarray(x[:, u0 + 3].reshape(P, BLOCKS)),
        "weights": weights,
        "params": params,
        "emb_area": np.ascontiguousarray(np.asarray(L0_rec_emb_area)),
    }
    nc = bacc.Bacc("TRN2", target_bir_lowering=False, num_devices=1)
    args = [nc.dram_tensor(name, a.shape, mybir.dt.from_np(a.dtype), kind="ExternalInput").ap()
            for name, a in arrays.items()]
    out = nc.dram_tensor("out", (P, BLOCKS), mybir.dt.float32, kind="ExternalOutput").ap()
    build(nc, *args, out)
    got = run_bass_kernel_spmd(nc, [arrays], core_ids=[0]).results[0]["out"]
    return got.reshape(BATCH, 1)
```

```python
import concourse.bass as bass
from concourse import mybir
from contextlib import ExitStack

P = 128
BATCH = 512
BLOCKS = BATCH // P
D = 32
HID = 64
BAG = D + 1
Z = HID + 1
GENRE, DIRECTOR, ACTOR = 25, 2186, 8030
AREA_ROWS = 3402
TABLES = (6, 2, 7, 21)
TROWS = sum(TABLES)

DIR_CHUNKS = DIRECTOR // P
DIR_REST = DIRECTOR - DIR_CHUNKS * P
ACT_CHUNKS = -(-ACTOR // P)
CHUNKS = 1 + DIR_CHUNKS + ACT_CHUNKS
STREAMED = CHUNKS - 1
GENRE_AT, TABLE_AT = 32, 64
PAIR = 2
assert STREAMED % PAIR == 0

A, B = 0, 1
PHASE_BLOCKS = (range(0, BLOCKS - 1), range(BLOCKS - 1, BLOCKS))
WIDTH = [len(b) * P for b in PHASE_BLOCKS]
FIRST = [b[0] * P for b in PHASE_BLOCKS]
X_AT = [BATCH, BATCH + STREAMED * WIDTH[A]]
X_COLS = BATCH + STREAMED * BATCH

SLOTS = 4
A_GROUP = 4
A_LOOPS = STREAMED // (A_GROUP * SLOTS)
A_BEFORE = 3
assert A_LOOPS * A_GROUP * SLOTS == STREAMED
B_LOADS = [16, 16, 16, 8, 8, 4, 4, 4, 2, 2]
assert sum(B_LOADS) == STREAMED
B_STEP = 4
B_STEPS = [min(B_STEP, n) for n in B_LOADS for _ in range(0, n, B_STEP)]

COLS = {"idx": (0, 4), "tables": (4, 4 + P), "w1_area": (0, HID), "r_genre": (HID, HID + Z)}
PCOLS = max(b for _, b in COLS.values())
for _name, _n in (("w1_tables", HID), ("r_director", Z), ("r_actor", Z), ("w2", Z), ("wout", Z)):
    COLS[_name] = (PCOLS, PCOLS + _n)
    PCOLS += _n


def chunk_at(phase, c):
    return X_AT[phase] + (c - 1) * WIDTH[phase]


def build(nc, x_rows, area_index, weights, params, emb_area, out):
    fp32 = mybir.dt.float32
    int32 = mybir.dt.int32
    ALU = mybir.AluOpType
    ACT = mybir.ActivationFunctionType

    with ExitStack() as ctx:
        def sb(name, shape, dt=fp32):
            return ctx.enter_context(nc.sbuf_tensor(name, shape, dt))

        def sem(name):
            return ctx.enter_context(nc.semaphore(name))

        x = sb("x", [P, X_COLS], fp32)
        x_int = x[:, :].bitcast(int32)
        w = sb("w", [P, CHUNKS * BAG])
        par = sb("par", [P, PCOLS])
        ident = sb("ident", [P, P])
        area_raw = sb("area_raw", [P, BLOCKS], int32)
        area_clamped = sb("area_clamped", [P, BLOCKS])
        area_wrap = sb("area_wrap", [P, BLOCKS])
        area_row = sb("area_row", [P, BLOCKS], int32)
        area_emb = sb("area_emb", [P, BLOCKS * D])
        area_t = sb("area_t", [BAG, BATCH])
        clamped = sb("clamped", [P, BATCH])
        is_row = sb("is_row", [P, BATCH])
        onehot = sb("onehot", [P, BATCH])
        table_t = sb("table_t", [P, BATCH])
        genre_sum = sb("genre_sum", [BAG, BATCH])
        director_sum = sb("director_sum", [P, BATCH])
        actor_sum = sb("actor_sum", [P, BATCH])
        recip = sb("recip", [P, 3, BLOCKS])
        h1 = sb("h1", [P, BLOCKS, HID])
        h1_t = sb("h1_t", [Z, BATCH])
        scored = sb("scored", [P, BLOCKS, Z])
        y = sb("y", [P, BLOCKS])

        bank = [ctx.enter_context(nc.psum_tensor(name, [P, BATCH], fp32)) for name in (
            "ps_actor_a", "ps_actor_b", "ps_director_a", "ps_director_b", "ps_genre", "ps_table", "ps_area", "ps_user")]
        ps_actor = bank[0:2]
        ps_director = bank[2:4]
        ps_genre, ps_table, ps_area, ps_user = bank[4:8]

        def blocks_of(t):
            return t[:, :].rearrange("p (c n) -> p c n", c=BLOCKS)

        ps_z = [blocks_of(ps_table), blocks_of(ps_user)]
        ps_h1 = [ps_genre, ps_area]
        ps_h2 = [blocks_of(ps_director[A]), blocks_of(ps_actor[A])]
        ps_user = blocks_of(ps_user)

        def col(name, rows=slice(0, P)):
            a, b = COLS[name]
            return par[rows, a:b]

        area_index_in = sem("area_index_in")
        params_in = sem("params_in")
        weights_in = [sem(f"weights_in{i}") for i in range(3)]
        mixed_in = sem("mixed_in")
        a_in = [sem(f"a_in{s}") for s in range(SLOTS)]
        b_in = [sem(f"b_in{i}") for i in range(len(B_LOADS))]
        x_float = sem("x_float")
        zeroed = sem("zeroed")
        ident_zero = sem("ident_zero")
        ident_ready = sem("ident_ready")
        area_step = sem("area_step")
        area_gathered = sem("area_gathered")
        hot_step = sem("hot_step")
        onehot_ready = sem("onehot_ready")
        table_picked = sem("table_picked")
        table_copied = sem("table_copied")
        area_turned = sem("area_turned")
        area_copied = sem("area_copied")
        user_done = sem("user_done")
        user_copied = sem("user_copied")
        genre_done = sem("genre_done")
        genre_copied = sem("genre_copied")
        director_done = sem("director_done")
        director_copied = sem("director_copied")
        actor_done = sem("actor_done")
        actor_copied = sem("actor_copied")
        z_done = [sem(f"z_done{bag}") for bag in range(3)]
        recip_done = [sem(f"recip_done{bag}") for bag in range(3)]
        mean_added = [sem(f"mean_added{bag}") for bag in range(3)]
        h1_turned = sem("h1_turned")
        h1_copied = sem("h1_copied")
        h2_done = sem("h2_done")
        scores_summed = sem("scores_summed")
        out_done = sem("out_done")

        W_PARTS = [0, 1 + DIR_CHUNKS, 1 + DIR_CHUNKS + ACT_CHUNKS // 2, CHUNKS]

        block = ctx.enter_context(nc.Block())

        @block.sync
        def _(sync):
            sync.dma_start(x_int[:, 0:BATCH], x_rows[:, 0:BATCH]).then_inc(mixed_in, 16)
            n = A_GROUP * WIDTH[A]
            for s in range(SLOTS):
                at = chunk_at(A, 1 + A_GROUP * s)
                sync.dma_start(x_int[:, at:at + n], x_rows[:, at:at + n]).then_inc(a_in[s], 16)
            with sync.Fori(1, A_LOOPS) as k:
                for s in range(SLOTS):
                    sync.wait_ge(a_in[s], k * 16)
                    at = k * (SLOTS * n) + chunk_at(A, 1 + A_GROUP * s)
                    sync.dma_start(x_int[:, bass.ds(at, n)], x_rows[:, bass.ds(at, n)]).then_inc(a_in[s], 16)
            c = 1
            for i, chunks in enumerate(B_LOADS):
                if i < SLOTS:
                    sync.wait_ge(a_in[i], A_LOOPS * 16)
                at, n = chunk_at(B, c), chunks * WIDTH[B]
                sync.dma_start(x_int[:, at:at + n], x_rows[:, at:at + n]).then_inc(b_in[i], 16)
                c += chunks
            sync.wait_ge(scores_summed, BLOCKS)
            sync.dma_start(out, y[:, :]).then_inc(out_done, 16)
            sync.wait_ge(out_done, 16)

        @block.scalar
        def _(act):
            act.dma_start(area_raw[:, :], area_index).then_inc(area_index_in, 16)
            act.dma_start(par[:, :], params).then_inc(params_in, 16)
            for i in range(3):
                a, b = W_PARTS[i] * BAG, W_PARTS[i + 1] * BAG
                act.dma_start(w[:, a:b], weights[:, a:b]).then_inc(weights_in[i], 16)
            act.wait_ge(table_picked, 1)
            nc.scalar.copy(table_t[:, :], ps_table[:, :]).then_inc(table_copied, 1)
            act.wait_ge(genre_done, 1)
            nc.scalar.copy(genre_sum[:, :], ps_genre[0:BAG, :]).then_inc(genre_copied, 1)
            act.wait_ge(area_turned, 1)
            nc.scalar.copy(area_t[0:D, :], ps_area[0:D, :]).then_inc(area_copied, 1)
            act.wait_ge(zeroed, 4)
            for phase in (A, B):
                cs = slice(FIRST[phase], FIRST[phase] + WIDTH[phase])
                act.wait_ge(director_done, phase + 1)
                for half in (0, 64):
                    nc.scalar.copy(director_sum[half:half + BAG, cs], ps_director[phase][half:half + BAG, 0:WIDTH[phase]])\
                        .then_inc(director_copied, 1)
                if phase == B:
                    act.wait_ge(h1_turned, 1)
                    nc.scalar.activation(h1_t[0:HID, 0:WIDTH[A]], ps_h1[A][0:HID, 0:WIDTH[A]], ACT.Relu)\
                        .then_inc(h1_copied, 1)
                act.wait_ge(actor_done, phase + 1)
                for half in (0, 64) if phase == A else (64,):
                    nc.scalar.copy(actor_sum[half:half + BAG, cs], ps_actor[phase][half:half + BAG, 0:WIDTH[phase]])\
                        .then_inc(actor_copied, 1)
            act.wait_ge(h1_turned, 2)
            nc.scalar.activation(h1_t[0:HID, FIRST[B]:BATCH], ps_h1[B][0:HID, 0:WIDTH[B]], ACT.Relu)\
                .then_inc(h1_copied, 1)

        @block.gpsimd
        def _(pool):
            pool.memset(ident[:, :], 0.0).then_inc(ident_zero, 1)
            pool.wait_ge(ident_zero, 1)
            pool.affine_select(out=ident[:, :], in_=ident[:, :], compare_op=ALU.not_equal, fill=1.0,
                               base=0, pattern=[[-1, P]], channel_multiplier=1).then_inc(ident_ready, 1)
            pool.memset(director_sum[:, :], 0.0).then_inc(zeroed, 1)
            pool.wait_ge(zeroed, 1)
            pool.memset(actor_sum[:, :], 0.0).then_inc(zeroed, 1)
            pool.wait_ge(zeroed, 2)
            pool.memset(area_t[D:D + 1, :], 1.0).then_inc(zeroed, 1)
            pool.wait_ge(zeroed, 3)
            pool.memset(h1_t[HID:HID + 1, :], 1.0).then_inc(zeroed, 1)
            pool.wait_ge(area_step, 3)
            for c in range(BLOCKS):
                pool.indirect_dma_start(area_emb[:, c * D:(c + 1) * D], None, emb_area,
                                        bass.IndirectOffsetOnAxis(ap=area_row[:, c:c + 1], axis=0))\
                    .then_inc(area_gathered, 16)

        @block.vector
        def _(dve):
            dve.wait_ge(area_index_in, 16)
            nc.vector.tensor_scalar(area_clamped[:, :], area_raw[:, :], float(-AREA_ROWS),
                                    float(AREA_ROWS - 1), ALU.max, ALU.min).then_inc(area_step, 1)
            dve.wait_ge(area_step, 1)
            nc.vector.tensor_scalar(area_wrap[:, :], area_clamped[:, :], 0.0, float(AREA_ROWS),
                                    ALU.is_lt, ALU.mult).then_inc(area_step, 1)
            dve.wait_ge(area_step, 2)
            nc.vector.tensor_tensor(area_row[:, :], area_clamped[:, :], area_wrap[:, :],
                                    ALU.add).then_inc(area_step, 1)

            dve.wait_ge(mixed_in, 16)
            nc.vector.tensor_copy(x[:, 0:BATCH], x_int[:, 0:BATCH]).then_inc(x_float, 1)
            dve.wait_ge(params_in, 16)
            dve.wait_ge(x_float, 1)
            rows = slice(TABLE_AT, TABLE_AT + TROWS)
            nc.vector.tensor_scalar(clamped[rows, :], x[rows, 0:BATCH], par[rows, 0:1], par[rows, 1:2],
                                    ALU.max, ALU.min).then_inc(hot_step, 1)
            dve.wait_ge(hot_step, 1)
            nc.vector.tensor_scalar(is_row[rows, :], clamped[rows, :], par[rows, 2:3], None,
                                    ALU.is_equal).then_inc(hot_step, 1)
            dve.wait_ge(hot_step, 2)
            nc.vector.scalar_tensor_tensor(onehot[rows, :], clamped[rows, :], par[rows, 3:4], is_row[rows, :],
                                           ALU.is_equal, ALU.add).then_inc(onehot_ready, 1)

            def convert_a(first, end):
                with dve.Fori(first, end) as k:
                    for s in range(SLOTS):
                        dve.wait_ge(a_in[s], k * 16 + 16)
                        for j in range(0, A_GROUP, PAIR):
                            at = k * (SLOTS * A_GROUP * WIDTH[A]) + chunk_at(A, 1 + A_GROUP * s + j)
                            n = PAIR * WIDTH[A]
                            nc.vector.tensor_copy(x[:, bass.ds(at, n)], x_int[:, bass.ds(at, n)]).then_inc(x_float, 1)

            def convert_b(loads):
                for i in loads:
                    dve.wait_ge(b_in[i], 16)
                    first = 1 + sum(B_LOADS[:i])
                    for c in range(first, first + B_LOADS[i], B_STEP):
                        at, n = chunk_at(B, c), min(B_STEP, B_LOADS[i]) * WIDTH[B]
                        nc.vector.tensor_copy(x[:, at:at + n], x_int[:, at:at + n]).then_inc(x_float, 1)

            def add_mean(bag, blocks, ps):
                a, b = blocks[0], blocks[-1] + 1
                dve.wait_ge(z_done[bag], b)
                nc.vector.reciprocal(recip[:, bag, a:b], ps[:, a:b, HID]).then_inc(recip_done[bag], 1)
                dve.wait_ge(recip_done[bag], 1 if bag == 0 or a == 0 else 2)
                if bag:
                    dve.wait_ge(mean_added[bag - 1], b)
                else:
                    dve.wait_ge(user_copied, 1)
                for c in blocks:
                    nc.vector.scalar_tensor_tensor(h1[:, c, :], ps[:, c, 0:HID], recip[:, bag, c:c + 1],
                                                   h1[:, c, :], ALU.mult, ALU.add).then_inc(mean_added[bag], 1)

            def sum_scores(phase):
                dve.wait_ge(h2_done, phase + 1)
                for c in PHASE_BLOCKS[phase]:
                    nc.vector.scalar_tensor_tensor(scored[:, c, :], ps_h2[phase][:, c, 0:Z], 0.0, col("wout"),
                                                   ALU.max, ALU.mult, accum_out=y[:, c:c + 1]).then_inc(scores_summed, 1)

            convert_a(0, A_BEFORE)
            dve.wait_ge(user_done, 1)
            nc.vector.tensor_copy(h1[:, :, :], ps_user[:, :, 0:HID]).then_inc(user_copied, 1)
            add_mean(0, range(BLOCKS), ps_z[A])
            add_mean(1, PHASE_BLOCKS[A], ps_z[A])
            convert_a(A_BEFORE, A_LOOPS)
            convert_b(range(0, 1))
            add_mean(2, PHASE_BLOCKS[A], ps_z[A])
            convert_b(range(1, 2))
            add_mean(1, PHASE_BLOCKS[B], ps_z[B])
            convert_b(range(2, 3))
            sum_scores(A)
            convert_b(range(3, len(B_LOADS)))
            dve.wait_ge(actor_done, 2)
            dve.wait_ge(zeroed, 2)
            nc.vector.tensor_copy(actor_sum[0:BAG, FIRST[B]:BATCH], ps_actor[B][0:BAG, 0:WIDTH[B]])\
                .then_inc(actor_copied, 1)
            add_mean(2, PHASE_BLOCKS[B], ps_z[B])
            sum_scores(B)

        @block.tensor
        def _(pe):
            def mixed(rows):
                return w[rows, 0:BAG], x[rows, 0:BATCH]

            def bag_chunk(phase, c):
                half = 64 * (c % 2)
                director = c <= DIR_CHUNKS
                ps = (ps_director if director else ps_actor)[phase]
                first = c == 1 if director else c <= DIR_CHUNKS + PAIR
                last = c > DIR_CHUNKS - PAIR if director else c > CHUNKS - 1 - PAIR
                at = chunk_at(phase, c)
                done = nc.tensor.matmul(ps[half:half + BAG, 0:WIDTH[phase]], w[:, c * BAG:(c + 1) * BAG],
                                        x[:, at:at + WIDTH[phase]], start=first, stop=last)
                if c == DIR_CHUNKS:
                    done.then_inc(director_done, 1)
                if c == CHUNKS - 1:
                    done.then_inc(actor_done, 1)

            pe.wait_ge(weights_in[0], 16)
            pe.wait_ge(x_float, 1)
            wt, xt = mixed(slice(GENRE_AT, GENRE_AT + 32))
            nc.tensor.matmul(ps_genre[0:BAG, :], wt, xt, start=True, stop=True).then_inc(genre_done, 1)
            assert DIR_REST <= GENRE_AT
            wt, xt = mixed(slice(0, GENRE_AT))
            for phase in (A, B):
                nc.tensor.matmul(ps_director[phase][0:BAG, 0:WIDTH[phase]], wt,
                                 xt[:, FIRST[phase]:FIRST[phase] + WIDTH[phase]], start=True, stop=False)
            pe.wait_ge(onehot_ready, 1)
            pe.wait_ge(params_in, 16)
            rows = slice(TABLE_AT, TABLE_AT + TROWS)
            nc.tensor.matmul(ps_table[:, :], col("tables", rows), onehot[rows, :],
                             start=True, stop=True).then_inc(table_picked, 1)

            def turn_area():
                pe.wait_ge(area_gathered, 16 * BLOCKS)
                pe.wait_ge(ident_ready, 1)
                for c in range(BLOCKS):
                    last = nc.tensor.transpose(ps_area[0:D, c * P:(c + 1) * P],
                                               area_emb[:, c * D:(c + 1) * D], ident[:, :])
                last.then_inc(area_turned, 1)

            def user_layer_one():
                pe.wait_ge(area_copied, 1)
                pe.wait_ge(zeroed, 4)
                pe.wait_ge(table_copied, 1)
                for c in range(BLOCKS):
                    cs = slice(c * P, (c + 1) * P)
                    nc.tensor.matmul(ps_user[:, c, 0:HID], area_t[:, cs], col("w1_area", slice(0, BAG)),
                                     start=True, stop=False)
                    last = nc.tensor.matmul(ps_user[:, c, 0:HID], table_t[:, cs], col("w1_tables"),
                                            start=False, stop=True)
                last.then_inc(user_done, 1)

            def bag_layer_one(bag, blocks, ps, sums, rows, r):
                for c in blocks:
                    nc.tensor.matmul(ps[:, c, 0:Z], sums[rows, c * P:(c + 1) * P], col(r, rows),
                                     start=True, stop=True).then_inc(z_done[bag], 1)

            def genre_layer_one():
                pe.wait_ge(genre_copied, 1)
                bag_layer_one(0, range(BLOCKS), ps_z[A], genre_sum, slice(0, BAG), "r_genre")

            both = slice(0, 64 + BAG)

            def director_layer_one(phase):
                pe.wait_ge(director_copied, 2 * phase + 2)
                if phase == A:
                    pe.wait_ge(mean_added[0], BLOCKS)
                else:
                    pe.wait_ge(user_copied, 1)
                bag_layer_one(1, PHASE_BLOCKS[phase], ps_z[phase], director_sum, both, "r_director")

            def actor_layer_one(phase):
                pe.wait_ge(actor_copied, 2 * phase + 2)
                pe.wait_ge(mean_added[1], PHASE_BLOCKS[phase][-1] + 1)
                bag_layer_one(2, PHASE_BLOCKS[phase], ps_z[phase], actor_sum, both, "r_actor")

            def turn_layer_one(phase):
                for c in PHASE_BLOCKS[phase]:
                    pe.wait_ge(mean_added[2], c + 1)
                    at = c * P - FIRST[phase]
                    last = nc.tensor.transpose(ps_h1[phase][0:HID, at:at + P], h1[:, c, :], ident[:, :])
                last.then_inc(h1_turned, 1)

            def layer_two(phase):
                pe.wait_ge(h1_copied, phase + 1)
                for c in PHASE_BLOCKS[phase]:
                    last = nc.tensor.matmul(ps_h2[phase][:, c, 0:Z], h1_t[:, c * P:(c + 1) * P],
                                            col("w2", slice(0, Z)), start=True, stop=True)
                last.then_inc(h2_done, 1)

            for c in range(1, CHUNKS, PAIR):
                pe.wait_ge(x_float, 1 + (c + 1) // PAIR)
                for chunk in range(c, c + PAIR):
                    if chunk in W_PARTS[1:3]:
                        pe.wait_ge(weights_in[W_PARTS.index(chunk)], 16)
                    bag_chunk(A, chunk)
                pairs_done = (c + 1) // PAIR
                if pairs_done == 14:
                    turn_area()
                if pairs_done == 18:
                    user_layer_one()
                    genre_layer_one()
                if pairs_done == 22:
                    director_layer_one(A)
            step, ends = 0, []
            for n in B_STEPS:
                step += n
                ends.append(step)
            for c in range(1, CHUNKS, PAIR):
                behind = [i for i, end in enumerate(ends) if end >= c + PAIR - 1][0]
                pe.wait_ge(x_float, 1 + STREAMED // PAIR + behind + 1)
                for chunk in range(c, c + PAIR):
                    bag_chunk(B, chunk)
                pairs_done = (c + 1) // PAIR
                if pairs_done == 4:
                    actor_layer_one(A)
                if pairs_done == 10:
                    turn_layer_one(A)
                if pairs_done == 12:
                    director_layer_one(B)
                if pairs_done == 16:
                    layer_two(A)
            actor_layer_one(B)
            turn_layer_one(B)
            layer_two(B)


def kernel(r_x, L0_rec_emb_rate, L0_rec_W_genre, L0_rec_W_director, L0_rec_W_actor, L0_rec_emb_gender,
           L0_rec_emb_age, L0_rec_emb_occ, L0_rec_emb_area, L0_rec_W1, L0_rec_b1, L0_rec_W2, L0_rec_b2,
           L0_rec_Wout, L0_rec_bout):
    import numpy as np
    import concourse.bacc as bacc
    from concourse import mybir
    from concourse.bass_utils import run_bass_kernel_spmd

    x = np.asarray(r_x)
    W1, W2 = np.asarray(L0_rec_W1), np.asarray(L0_rec_W2)
    xt = x.reshape(P, BLOCKS, x.shape[1]).transpose(2, 1, 0).reshape(x.shape[1], BATCH)
    d0, a0, u0 = 1 + GENRE, 1 + GENRE + DIRECTOR, 1 + GENRE + DIRECTOR + ACTOR

    rows = np.zeros((CHUNKS * P, BATCH), x.dtype)
    rows[0:DIR_REST] = xt[d0 + DIR_CHUNKS * P:a0]
    rows[GENRE_AT:GENRE_AT + GENRE] = xt[1:d0]
    at = TABLE_AT
    for n, source in zip(TABLES, (0, u0, u0 + 1, u0 + 2)):
        rows[at:at + n] = xt[source]
        at += n
    rows[P:P + DIR_CHUNKS * P] = xt[d0:d0 + DIR_CHUNKS * P]
    rows[P + DIR_CHUNKS * P:P + DIR_CHUNKS * P + ACTOR] = xt[a0:u0]
    rows = rows.reshape(CHUNKS, P, BATCH).transpose(1, 0, 2)
    x_rows = np.concatenate([rows[:, 0]] + [
        rows[:, 1:, FIRST[phase]:FIRST[phase] + WIDTH[phase]].reshape(P, STREAMED * WIDTH[phase])
        for phase in (A, B)], axis=1)

    wt = np.zeros((CHUNKS * P, BAG), W1.dtype)
    wt[:, D] = 1.0
    wd = np.asarray(L0_rec_W_director).T
    wt[0:DIR_REST, 0:D] = wd[DIR_CHUNKS * P:]
    wt[GENRE_AT:GENRE_AT + GENRE, 0:D] = np.asarray(L0_rec_W_genre).T
    wt[P:P + DIR_CHUNKS * P, 0:D] = wd[0:DIR_CHUNKS * P]
    wt[P + DIR_CHUNKS * P:P + DIR_CHUNKS * P + ACTOR, 0:D] = np.asarray(L0_rec_W_actor).T
    weights = np.ascontiguousarray(wt.reshape(CHUNKS, P, BAG).transpose(1, 0, 2)).reshape(P, CHUNKS * BAG)

    params = np.zeros((P, PCOLS), W1.dtype)

    def put(name, row, block):
        a = COLS[name][0]
        params[row:row + block.shape[0], a:a + block.shape[1]] = block

    tables = (L0_rec_emb_rate, L0_rec_emb_gender, L0_rec_emb_age, L0_rec_emb_occ)
    w1_at = (0, 4 * D, 5 * D, 6 * D)
    row = TABLE_AT
    for t, n in enumerate(TABLES):
        for j in range(n):
            params[row + j, 0:4] = (-n, n - 1, j, j - n)
        params[row:row + n, COLS["tables"][0] + t * D:COLS["tables"][0] + (t + 1) * D] = np.asarray(tables[t])
        put("w1_tables", t * D, W1[:, w1_at[t]:w1_at[t] + D].T)
        row += n
    put("w1_area", 0, W1[:, 7 * D:8 * D].T)
    put("w1_area", D, np.asarray(L0_rec_b1).reshape(1, HID))
    for name, block, halves in (("r_genre", 1, (0,)), ("r_director", 2, (0, 64)), ("r_actor", 3, (0, 64))):
        for half in halves:
            put(name, half, W1[:, block * D:(block + 1) * D].T)
            params[half + D, COLS[name][0] + HID] = 1.0
    put("w2", 0, W2.T)
    put("w2", HID, np.asarray(L0_rec_b2).reshape(1, HID))
    params[HID, COLS["w2"][1] - 1] = 1.0
    params[:, COLS["wout"][0]:COLS["wout"][1] - 1] = np.asarray(L0_rec_Wout)
    params[:, COLS["wout"][1] - 1] = np.asarray(L0_rec_bout)

    arrays = {
        "x_rows": x_rows,
        "area_index": np.ascontiguousarray(x[:, u0 + 3].reshape(P, BLOCKS)),
        "weights": weights,
        "params": params,
        "emb_area": np.ascontiguousarray(np.asarray(L0_rec_emb_area)),
    }
    nc = bacc.Bacc("TRN2", target_bir_lowering=False, num_devices=1)
    args = [nc.dram_tensor(name, a.shape, mybir.dt.from_np(a.dtype), kind="ExternalInput").ap()
            for name, a in arrays.items()]
    out = nc.dram_tensor("out", (P, BLOCKS), mybir.dt.float32, kind="ExternalOutput").ap()
    build(nc, *args, out)
    got = run_bass_kernel_spmd(nc, [arrays], core_ids=[0]).results[0]["out"]
    return got.reshape(BATCH, 1)
```
